# Optimizing a Trainium2 kernel written in Bass

```python
import numpy as np
import jax
import jax.numpy as jnp

def _softmax(x, axis=-1):
    return jax.nn.softmax(x, axis=axis)

def _gelu(x):
    return jax.nn.gelu(x, approximate=True)

def _silu(x):
    return jax.nn.silu(x)

def _sigmoid(x):
    return jax.nn.sigmoid(x)

def _layernorm(x, axis=-1, eps=1e-05):
    m = jnp.mean(x, axis=axis, keepdims=True)
    v = jnp.var(x, axis=axis, keepdims=True)
    return (x - m) / jnp.sqrt(v + eps)

def _scatter_add(tgt, idx, src, axis=0):
    return tgt.at[idx].add(src)

def _segment_sum(src, seg, n):
    return jax.ops.segment_sum(src, seg, n)
kernel_name = 'mk_recurrent_d1_jaxref_r8_dbb3de'

def setup_inputs(seed: int=0):
    np.random.seed(seed)
    _w = jnp.asarray

    def _L0_attn_setup():
        import jax, jax.numpy as jnp
        import numpy as np
        D_MODEL, NUM_HEADS, D_HEAD, SEQ, BATCH = (128, 16, 64, 512, 1)
        key = jax.random.key(seed)
        ks = jax.random.split(key, 5)
        scale = 1.0 / np.sqrt(D_MODEL)
        x = jax.random.normal(ks[0], (BATCH, SEQ, D_MODEL), dtype=jnp.float32)
        W_K = jax.random.normal(ks[1], (NUM_HEADS, D_HEAD, D_MODEL), dtype=jnp.float32) * scale
        W_Q = jax.random.normal(ks[2], (NUM_HEADS, D_HEAD, D_MODEL), dtype=jnp.float32) * scale
        W_V = jax.random.normal(ks[3], (NUM_HEADS, D_HEAD, D_MODEL), dtype=jnp.float32) * scale
        W_O = jax.random.normal(ks[4], (D_MODEL, NUM_HEADS * D_HEAD), dtype=jnp.float32) * scale
        return {'x': x, 'W_K': W_K, 'W_Q': W_Q, 'W_V': W_V, 'W_O': W_O}
    _L0_attn_in = _L0_attn_setup()

    def _L0_ffn_setup():
        import jax, jax.numpy as jnp
        import numpy as np
        HIDDEN = 128
        INTER = 512
        key = jax.random.key(seed)
        k1, k2, k3, k4, k5 = jax.random.split(key, 5)
        hidden_states = jax.random.normal(k1, (4, 256, HIDDEN), dtype=jnp.float32)
        W1 = jax.random.normal(k2, (HIDDEN, INTER), dtype=jnp.float32) * (1.0 / np.sqrt(HIDDEN))
        b1 = jax.random.normal(k3, (INTER,), dtype=jnp.float32) * 0.02
        W2 = jax.random.normal(k4, (INTER, HIDDEN), dtype=jnp.float32) * (1.0 / np.sqrt(INTER))
        b2 = jax.random.normal(k5, (HIDDEN,), dtype=jnp.float32) * 0.02
        return {'hidden_states': hidden_states, 'W1': W1, 'b1': b1, 'W2': W2, 'b2': b2}
    _L0_ffn_in = _L0_ffn_setup()
    _d = {'L0_attn_x': _L0_attn_in['x'], 'L0_attn_W_K': _L0_attn_in['W_K'], 'L0_attn_W_Q': _L0_attn_in['W_Q'], 'L0_attn_W_V': _L0_attn_in['W_V'], 'L0_attn_W_O': _L0_attn_in['W_O'], 'L0_ffn_W1': _L0_ffn_in['W1'], 'L0_ffn_b1': _L0_ffn_in['b1'], 'L0_ffn_W2': _L0_ffn_in['W2'], 'L0_ffn_b2': _L0_ffn_in['b2']}
    _x0 = _d['L0_attn_x']
    _d['L0_attn_x'] = jax.random.normal(jax.random.fold_in(jax.random.key(seed), 1), (4, 1024, 128), dtype=_x0.dtype)
    del _x0
    return _d

def reference(L0_attn_x, L0_attn_W_K, L0_attn_W_Q, L0_attn_W_V, L0_attn_W_O, L0_ffn_W1, L0_ffn_b1, L0_ffn_W2, L0_ffn_b2):

    def _L0_attn_ref(x, W_K, W_Q, W_V, W_O):
        import jax, jax.numpy as jnp
        import numpy as np
        D_MODEL, NUM_HEADS, D_HEAD, SEQ, BATCH = (128, 16, 64, 512, 1)
        B, S, D = x.shape
        d_head = W_K.shape[1]
        k = jnp.einsum('ihd,bpd->biph', W_K, x)
        q = jnp.einsum('ihd,bpd->biph', W_Q, x)
        v = jnp.einsum('ihd,bpd->biph', W_V, x)
        scores = jnp.einsum('biph,biqh->biqp', k, q)
        mask = jnp.tril(jnp.ones((S, S), dtype=x.dtype))
        scores_masked = jnp.tril(scores) - 10000000000.0 * (1.0 - mask)
        attn = jax.nn.softmax(scores_masked / np.sqrt(d_head), axis=-1)
        z = jnp.einsum('biph,biqp->biqh', v, attn)
        z_flat = jnp.transpose(z, (0, 2, 1, 3)).reshape(B, S, -1)
        out = jnp.einsum('df,bqf->bqd', W_O, z_flat)
        return out

    def _L0_ffn_ref(hidden_states, W1, b1, W2, b2):
        import jax, jax.numpy as jnp
        import numpy as np
        HIDDEN = 128
        INTER = 512
        h = jax.nn.relu(jnp.einsum('bsh,hi->bsi', hidden_states, W1) + b1)
        return jnp.einsum('bsi,ih->bsh', h, W2) + b2
    x = L0_attn_x
    xn = _layernorm(x, axis=-1)
    s = _L0_attn_ref(xn, L0_attn_W_K, L0_attn_W_Q, L0_attn_W_V, L0_attn_W_O)
    g = _silu(_L0_ffn_ref(xn, L0_ffn_W1, L0_ffn_b1, L0_ffn_W2, L0_ffn_b2))
    x = x + s * g
    return x

_drawn_inputs = setup_inputs


def setup_inputs(seed=0):
    import zlib

    import numpy as np

    out = dict(_drawn_inputs(seed))
    spreads = {}
    factors = {'L0_ffn_b1': 8.0, 'L0_ffn_b2': 8.0}
    for name, (base, spread) in spreads.items():
        noise = np.random.default_rng([zlib.crc32(name.encode()), seed]).standard_normal(out[name].shape)
        drawn = base * np.exp(spread * noise) if base else spread * noise
        out[name] = jnp.asarray(drawn.astype(out[name].dtype))
    for name, factor in factors.items():
        out[name] = (out[name] * factor).astype(out[name].dtype)
    return out
```

```python
from contextlib import ExitStack

import concourse.bass as bass
from concourse import mybir
from concourse.alu_op_type import AluOpType as ALU

F32 = mybir.dt.float32
F32R = mybir.dt.float32r
BF16 = mybir.dt.bfloat16
ACT = mybir.ActivationFunctionType
AX_X = mybir.AxisListType.X

P = 128
BANK = 512
MASKED = -1.0e10
EPS = 1e-5


class Tally:

    def __init__(self, lead, body, not_first=(), not_last=(), tail=()):
        self.lead, self.tail = list(lead), list(tail)
        self.first = [e for e in body if e not in not_first]
        self.body = list(body)
        self.last = [e for e in body if e not in not_last]

    def upto(self, turn, event):
        if turn.kind == "lead":
            return self.lead.index(event) + 1
        if turn.kind == "first":
            return len(self.lead) + self.first.index(event) + 1
        done = len(self.lead) + len(self.first)
        if turn.kind == "tail":
            return (done + (turn.it - 2) * len(self.body) + len(self.last)
                    + self.tail.index(event) + 1)
        events = self.last if turn.kind == "last" else self.body
        return (turn.it - 1) * len(self.body) + (done + events.index(event) + 1)


class Turn:

    def __init__(self, it, kind):
        self.it, self.kind = it, kind


def attention_gated_by_ffn(nc, x, x_t, wq_t, wk_t, wv_t, wo_t, w1, b1, w2, b2, out_t):
    TOKENS, D = x.shape
    HEADS_DIM = wq_t.shape[1]
    FF = w1.shape[1]
    DH = 64
    SEQ = 1024
    BATCHES = TOKENS // SEQ
    PAIRS = HEADS_DIM // P
    QUADS = BATCHES * PAIRS // 2
    PER_BATCH = QUADS // BATCHES
    TILES = TOKENS // P
    SEQ_TILES = SEQ // P
    FC = FF // P
    FT = TOKENS // QUADS
    SCALE = 1.0 / 8.0
    assert D == P and DH * 2 == P and SCALE == DH ** -0.5 and FC * FT == 2 * BANK

    M_BODY = [(0, "R"), (0, "W1a"), (0, "W1b"), (0, "O"), (1, "R"), (1, "V0"), (1, "V1"), (1, "O"),
              (2, "R"), (2, "W2"), (2, "O"), (3, "R"), (3, "V0"), (3, "V1"), (3, "O")]
    M_USES = Tally(["V0", "V1"], M_BODY, not_first=[(0, "R"), (0, "O")],
                   not_last=[(3, "V0"), (3, "V1")], tail=["R", "O"])

    with ExitStack() as ctx:
        def sb(name, shape, dt=F32):
            return ctx.enter_context(nc.sbuf_tensor(name, shape, dt))

        def psum(name, shape):
            return ctx.enter_context(nc.psum_tensor(name, shape, F32))

        def sem(name):
            return ctx.enter_context(nc.semaphore(name))

        xn_dram = nc.dram_tensor("xn_full", [P, TOKENS], F32, kind="Internal").ap()
        xn_hi_dram = nc.dram_tensor("xn_hi", [P, TOKENS], F32, kind="Internal").ap()
        xn_lo_dram = nc.dram_tensor("xn_lo", [P, TOKENS], F32, kind="Internal").ap()

        xn = [sb(f"xn{i}", [P, SEQ]) for i in (0, 1)]
        xh = [sb(f"xh{i}", [P, SEQ], F32R) for i in (0, 1)]
        xl = [sb(f"xl{i}", [P, SEQ], F32R) for i in (0, 1)]
        w_raw = [sb(f"w_raw{i}", [P, 3 * P]) for i in (0, 1)]
        w_hi = [sb(f"w_hi{i}", [P, 3 * P], F32R) for i in (0, 1)]
        w_lo = [sb(f"w_lo{i}", [P, 3 * P], F32R) for i in (0, 1)]
        wv = [sb(f"wv{i}", [P, P]) for i in (0, 1)]
        wo = [sb(f"wo{i}", [P, P]) for i in (0, 1)]
        q_hi = [sb(f"q_hi{i}", [P, 2, SEQ], F32R) for i in (0, 1)]
        q_lo = [sb(f"q_lo{i}", [P, 2, SEQ], F32R) for i in (0, 1)]
        k_st = [sb(f"k_st{i}", [P, 2, SEQ], F32R) for i in (0, 1)]
        v = [sb(f"v{i}", [P, SEQ_TILES, P]) for i in (0, 1)]
        prob = [sb(f"prob{i}", [P, SEQ]) for i in (0, 1)]
        prob_t = [sb("prob_t0", [P, 2, 4, BANK]), sb("prob_t1", [P, 2, 8, BANK])]
        neg_max = sb("neg_max", [P, 2, 8])
        row_sum = sb("row_sum", [P, 2, 8])
        recip = sb("recip", [P, 8])
        recip_wide = sb("recip_wide", [P, 8, DH])
        recip_t = sb("recip_t", [P, BANK])
        z = sb("z", [P, BANK])
        s_t = sb("s_t", [P, TOKENS])
        g_t = sb("g_t", [P, TOKENS])
        w1_raw = sb("w1_raw", [P, FF])
        w1_hi = sb("w1_hi", [P, FF], F32R)
        w1_lo = sb("w1_lo", [P, FF], F32R)
        w2_sb = sb("w2_sb", [P, FC, P])
        b1_sb = sb("b1_sb", [P, FC])
        b2_sb = sb("b2_sb", [P, 2])
        xf_hi = sb("xf_hi", [P, FT], F32R)
        xf_lo = sb("xf_lo", [P, FT], F32R)
        h_sb = sb("h_sb", [P, FC, FT])
        sig = sb("sig", [P, 2, FT])
        ident = sb("ident", [P, P])
        ident_b = sb("ident_b", [P, P], BF16)
        mask_b = sb("mask_b", [P, P], BF16)
        stats = sb("stats", [P, TILES, 6])
        mean_var = sb("mean_var", [P, TILES, 2])
        rstd = sb("rstd", [P, TILES])
        eps_sb = sb("eps_sb", [P, 1])
        x_nat = prob_t[1][:, :, :, :].rearrange("p h j q -> p (h j q)")[:, 0:TOKENS].rearrange(
            "p (t d) -> p t d", d=D)
        stage = prob_t[0][:, :, :, :].rearrange("p h j q -> p (h j) q")
        x_t_sb = prob_t[0][:, :, :, :].rearrange("p h j q -> p (h j q)")

        score = [psum(f"score{i}", [P, 2 * BANK]) for i in (0, 1)]
        turned = [psum(f"turned{i}", [P, BANK]) for i in (0, 1)]
        z_ps = psum("z_ps", [P, BANK])
        m_ps = psum("m_ps", [P, BANK])
        x_ps = [score[i][:, BANK:2 * BANK] for i in (0, 1)]

        x_in = [sem(f"x_in{b}") for b in range(BATCHES)]
        const_in = sem("const_in")
        const_ready = sem("const_ready")
        zeroed = sem("zeroed")
        s_zeroed = sem("s_zeroed")
        stats_done = sem("stats_done")
        var_ready = sem("var_ready")
        std_ready = sem("std_ready")
        rstd_ready = sem("rstd_ready")
        xn_ready = sem("xn_ready")
        xt_full = sem("xt_full")
        xt_hi_done = sem("xt_hi_done")
        xt_lo_done = sem("xt_lo_done")
        xn_out = [sem(f"xn_out{n}") for n in range(TILES // 4)]
        w1_hi_done = sem("w1_hi_done")
        w1_done = sem("w1_done")
        b2_done = sem("b2_done")
        set_in = [sem(f"set_in{i}") for i in (0, 1)]
        wo_in = [sem(f"wo_in{i}") for i in (0, 1)]
        xf_in = sem("xf_in")
        w_hi_done = sem("w_hi_done")
        w_lo_done = sem("w_lo_done")
        x_full = [sem(f"x_full{i}") for i in (0, 1)]
        x_hi = [sem(f"x_hi{i}") for i in (0, 1)]
        x_free = [sem(f"x_free{i}") for i in (0, 1)]
        scored = sem("scored")
        max_done = sem("max_done")
        exp_done = sem("exp_done")
        turn_full = [sem(f"turn_full{i}") for i in (0, 1)]
        turn_free = [sem(f"turn_free{i}") for i in (0, 1)]
        recip_chain = sem("recip_chain")
        recip_ready = sem("recip_ready")
        pv_done = sem("pv_done")
        recip_t_done = sem("recip_t_done")
        z_done = sem("z_done")
        m_full = sem("m_full")
        m_free = sem("m_free")
        gate_exp = sem("gate_exp")
        gate_chain = sem("gate_chain")
        xt_in = sem("xt_in")
        fin_chain = sem("fin_chain")
        fin_ready = sem("fin_ready")
        out_done = sem("out_done")
        SET_DMAS = 7 * 16

        block = ctx.enter_context(nc.Block())

        def coords(u, n):
            par, blk, il, h = u // 2, u % 2, n // 2, n % 2
            return par, blk, il, h, 4 * blk + il + 1

        def groups(u, n):
            _, blk, _, _, tiles = coords(u, n)
            if blk == 0:
                return [(n % 2, 0, tiles)]
            return [(0, 0, 4), (1, 4, tiles - 4)]

        TURNS_OF = [[sum(1 for n in range(8) for g in groups(u, n) if g[0] == i) for u in range(4)]
                    for i in (0, 1)]
        TURNS = sum(TURNS_OF[0])
        assert TURNS == sum(TURNS_OF[1])

        def turns_before(t, u, n, bank):
            k = sum(TURNS_OF[bank][:u]) + sum(1 for m in range(n) for g in groups(u, m) if g[0] == bank)
            return t.it * TURNS + k

        PREP = [("K", 0), ("K", 1), ("Q", 0, 0), ("Q", 1, 0), ("Q", 0, 1), ("Q", 1, 1)]

        def preps_before(t, u, s):
            return t.it * 6 + (3 + (u // 2) * 3 + s // 2)

        def step_no(t, u, n):
            return t.it * 32 + (u * 8 + n)

        def unit_no(t, u):
            return t.it * 4 + u

        def batch_of(quad):
            return quad // PER_BATCH

        def pair_of(quad, par):
            return (quad % PER_BATCH) * 2 + par

        def next_quad(t):
            return t.it + 1

        def run(engine, body):
            body(Turn(0, "first"))
            with engine.Fori(1, QUADS - 1) as it:
                body(Turn(it, "mid"))
            body(Turn(QUADS - 1, "last"))

        END = Turn(QUADS, "tail")

        @block.sync
        def _(sp):
            xv = x.rearrange("(t p) d -> p t d", p=P)

            def load_set(par, quad):
                tok = bass.ds(batch_of(quad) * SEQ, SEQ)
                col = bass.ds(pair_of(quad, par) * P, P)
                sp.dma_start(xh[par][:, :].bitcast(F32), xn_hi_dram[:, tok]).then_inc(set_in[par], 16)
                sp.dma_start(xl[par][:, :].bitcast(F32), xn_lo_dram[:, tok]).then_inc(set_in[par], 16)
                sp.dma_start(xn[par][:, :], xn_dram[:, tok]).then_inc(set_in[par], 16)
                two = w_raw[par][:, 0:2 * P].rearrange("p (h r c) -> p r h c", h=2, r=2)
                for r in (0, 1):
                    sp.dma_start(two[:, r], wq_t[:, col].rearrange("p (h c) -> p h c", h=2))\
                      .then_inc(set_in[par], 16)
                sp.dma_start(w_raw[par][:, 2 * P:3 * P], wk_t[:, col]).then_inc(set_in[par], 16)
                sp.dma_start(wv[par][:, :], wv_t[:, col]).then_inc(set_in[par], 16)

            def load_wo(par, quad):
                sp.dma_start(wo[par][:, :], wo_t[bass.ds(pair_of(quad, par) * P, P), :])\
                  .then_inc(wo_in[par], 16)

            def load_xf(quad):
                tok = bass.ds(quad * FT, FT)
                sp.dma_start(xf_hi[:, :].bitcast(F32), xn_hi_dram[:, tok]).then_inc(xf_in, 16)
                sp.dma_start(xf_lo[:, :].bitcast(F32), xn_lo_dram[:, tok]).then_inc(xf_in, 16)

            for b in range(BATCHES):
                ts = slice(b * SEQ_TILES, (b + 1) * SEQ_TILES)
                sp.dma_start(x_nat[:, ts, :], xv[:, ts, :]).then_inc(x_in[b], 16)
            sp.dma_start(w1_raw[:, :], w1).then_inc(const_in, 16)
            sp.dma_start(w2_sb[:, :, :], w2.rearrange("(c p) d -> p c d", p=P)).then_inc(const_in, 16)
            with nc.allow_non_contiguous_dma(reason="two small vectors"):
                sp.dma_start(b1_sb[:, :], b1.rearrange("(c p) -> p c", p=P)).then_inc(const_in, 16)
                sp.dma_start(b2_sb[:, 0:1], b2.rearrange("(p a) -> p a", a=1)).then_inc(const_in, 16)
            for b in range(BATCHES):
                for c in range(2):
                    n = 2 * b + c
                    sp.wait_ge(xt_lo_done, n + 1)
                    tok = slice(n * BANK, (n + 1) * BANK)
                    st = 3 * (n % 2)
                    sp.dma_start(xn_dram[:, tok], stage[:, st, :]).then_inc(xn_out[n], 16)
                    sp.dma_start(xn_hi_dram[:, tok], stage[:, st + 1, :]).then_inc(xn_out[n], 16)
                    sp.dma_start(xn_lo_dram[:, tok], stage[:, st + 2, :]).then_inc(xn_out[n], 16)
                if b == 0:
                    for g in (0, 1):
                        sp.wait_ge(xn_out[g], 48)
                    load_set(0, 0)
                    load_set(1, 0)
                    load_xf(0)
                    load_wo(0, 0)
                    load_wo(1, 0)
            for g in range(2, TILES // 4):
                sp.wait_ge(xn_out[g], 48)

            def body(t):
                if t.kind != "last":
                    if t.kind == "first":
                        sp.wait_ge(m_full, 2)
                    else:
                        sp.wait_ge(m_full, M_USES.upto(t, (0, "R")) - 1)
                    load_set(0, next_quad(t))
                if t.kind != "first":
                    sp.wait_ge(m_full, M_USES.upto(t, (0, "O")))
                    load_wo(1, t.it)
                if t.kind != "last":
                    sp.wait_ge(m_full, M_USES.upto(t, (0, "W1b")))
                    load_xf(next_quad(t))
                    sp.wait_ge(m_full, M_USES.upto(t, (1, "V1")))
                    load_set(1, next_quad(t))
                    sp.wait_ge(m_full, M_USES.upto(t, (2, "O")))
                    load_wo(0, next_quad(t))

            run(sp, body)
            sp.wait_ge(pv_done, 4 * QUADS - 1)
            sp.dma_start(x_t_sb, x_t).then_inc(xt_in, 16)
            for c in range(TOKENS // SEQ):
                sp.wait_ge(fin_ready, c + 1)
                tok = slice(c * SEQ, (c + 1) * SEQ)
                sp.dma_start(out_t[:, tok], g_t[:, tok]).then_inc(out_done, 16)
            sp.wait_ge(out_done, 16 * (TOKENS // SEQ))

        @block.gpsimd
        def _(pool):
            nc.gpsimd.memset(ident[:, :], 0.0).then_inc(zeroed, 1)
            nc.gpsimd.memset(ident_b[:, :], 0.0).then_inc(zeroed, 1)
            nc.gpsimd.memset(mask_b[:, :], 0.0).then_inc(zeroed, 1)
            nc.gpsimd.memset(eps_sb[:, :], EPS).then_inc(zeroed, 1)
            pool.wait_ge(zeroed, 4)
            for m in (ident, ident_b):
                nc.gpsimd.affine_select(out=m[:, :], in_=m[:, :], compare_op=ALU.not_equal, fill=1.0,
                                        base=0, pattern=[[-1, P]], channel_multiplier=1)\
                  .then_inc(const_ready, 1)
            nc.gpsimd.affine_select(out=mask_b[:, :], in_=mask_b[:, :], compare_op=ALU.is_ge,
                                    fill=MASKED * SCALE, base=0, pattern=[[-1, P]],
                                    channel_multiplier=1).then_inc(const_ready, 1)
            nc.gpsimd.memset(s_t[:, :], 0.0).then_inc(s_zeroed, 1)

        @block.tensor
        def _(pe):
            mm = nc.tensor.matmul

            def three_passes(out, w, cols, hi, lo):
                w_h, w_l = w
                mm(out, w_h[:, cols], hi, start=True, stop=False)
                mm(out, w_h[:, cols], lo, start=False, stop=False)
                return mm(out, w_l[:, cols], hi, start=False, stop=True)

            def scores(u, n):
                par, blk, il, h, tiles = coords(u, n)
                q0 = (4 * blk + il) * P
                diag = score[n % 2][:, (tiles - 1) * P:tiles * P]
                lo, hi = 0, tiles * P
                for c0 in range(0, hi, BANK):
                    width = max(min(hi - c0, BANK), 2 * P)
                    dst = score[n % 2][:, c0:c0 + width]
                    keys = k_st[par][:, h, c0:c0 + width]
                    on_diag = c0 + BANK >= hi
                    mm(dst, q_hi[par][:, h, q0:q0 + P], keys, start=True, stop=False)
                    last = mm(dst, q_lo[par][:, h, q0:q0 + P], keys, start=False, stop=not on_diag)
                last = mm(diag, ident_b[:, :], mask_b[:, :], start=False, stop=True)
                last.then_inc(scored, 1)

            def turn_step(t, u, n):
                pe.wait_ge(exp_done, step_no(t, u, n) + 1)
                for bank, j0, count in groups(u, n):
                    before = turns_before(t, u, n, bank)
                    if not (t.kind == "first" and before == 0):
                        pe.wait_ge(turn_free[bank], before)
                    for j in range(count):
                        last = nc.tensor.transpose(turned[bank][:, j * P:(j + 1) * P],
                                                   prob[n % 2][:, (j0 + j) * P:(j0 + j + 1) * P],
                                                   ident[:, :])
                    last.then_inc(turn_full[bank], 1)

            def project(t, u, s):
                par = 1 if u == 0 else 0
                bank, what = s % 2, PREP[s]
                tok = slice(what[-1] * BANK, (what[-1] + 1) * BANK)
                before = s // 2 if u < 0 else preps_before(t, u, s)
                if not (u < 0 and before == 0):
                    pe.wait_ge(x_free[bank], before)
                if s == 0:
                    if u < 0:
                        pe.wait_ge(set_in[0], SET_DMAS)
                        pe.wait_ge(w_lo_done, 1)
                    else:
                        pe.wait_ge(set_in[par], (t.it + (1 if u == 0 else 2)) * SET_DMAS)
                        pe.wait_ge(w_lo_done, t.it * 2 + (2 if u == 0 else 3))
                cols = slice(2 * P, 3 * P) if what[0] == "K" else slice(what[1] * P, (what[1] + 1) * P)
                three_passes(x_ps[bank], (w_hi[par], w_lo[par]), cols, xh[par][:, tok], xl[par][:, tok])\
                    .then_inc(x_full[bank], 1)

            def use_m(t, key):
                pe.wait_ge(m_free, M_USES.upto(t, key) - 1)

            def project_v(par, half):
                for i in range(4):
                    j = 4 * half + i
                    last = mm(m_ps[:, i * P:(i + 1) * P], xn[par][:, j * P:(j + 1) * P], wv[par][:, :],
                              start=True, stop=True)
                last.then_inc(m_full, 1)

            def ffn_up(c0):
                for c in (c0, c0 + 1):
                    last = three_passes(m_ps[:, (c - c0) * FT:(c - c0 + 1) * FT], (w1_hi, w1_lo),
                                        slice(c * P, (c + 1) * P), xf_hi[:, :], xf_lo[:, :])
                last.then_inc(m_full, 1)

            def ffn_down():
                for c in range(FC):
                    last = mm(m_ps[:, 0:FT], w2_sb[:, c, :], h_sb[:, c, :], start=(c == 0), stop=(c == FC - 1))
                last.then_inc(m_full, 1)

            def turn_recip(units_done):
                pe.wait_ge(recip_ready, units_done)
                for il in range(4):
                    last = nc.tensor.transpose(m_ps[:, il * P:(il + 1) * P],
                                               recip_wide[:, 2 * il:2 * il + 2, :].rearrange("p h c -> p (h c)"),
                                               ident[:, :])
                last.then_inc(m_full, 1)

            def times_v(u, js):
                par, blk = u // 2, u % 2
                count = 4 * (blk + 1)
                for j in js:
                    q0 = max(0, j - 4 * blk) * P
                    for h in (0, 1):
                        last = mm(z_ps[h * DH:(h + 1) * DH, q0:BANK], v[par][:, j, h * DH:(h + 1) * DH],
                                  prob_t[blk][:, h, j, q0:BANK], start=(j == 0), stop=(j == count - 1))
                if js[-1] == count - 1:
                    last.then_inc(pv_done, 1)

            def before_times_v(t, units_done, copies):
                for i in (0, 1):
                    pe.wait_ge(turn_free[i], copies[i])
                if not (t.kind == "first" and units_done == 1):
                    pe.wait_ge(z_done, units_done - 1)

            def project_o(units_done, par, wo_count):
                pe.wait_ge(wo_in[par], wo_count * 16)
                pe.wait_ge(z_done, units_done)
                mm(m_ps[:, :], wo[par][:, :], z[:, :], start=True, stop=True).then_inc(m_full, 1)

            pe.wait_ge(const_ready, 3)
            for n in range(TILES // 4):
                pe.wait_ge(xn_ready, 4 * (n + 1))
                if n >= 2:
                    pe.wait_ge(xt_lo_done, n - 1)
                for i in range(4):
                    last = nc.tensor.transpose(turned[n % 2][:, i * P:(i + 1) * P], x_nat[:, 4 * n + i, :],
                                               ident[:, :])
                last.then_inc(xt_full, 1)
            for s in range(6):
                project(None, -1, s)
            for half in (0, 1):
                if half:
                    pe.wait_ge(m_free, 1)
                project_v(0, half)
            for i in (0, 1):
                pe.wait_ge(x_free[i], 3)
            pe.wait_ge(xt_lo_done, TILES // 4)
            scores(0, 0)

            def body(t):
                for u in range(4):
                    par, blk = u // 2, u % 2
                    prev = (u - 1) % 4
                    has_prev = not (t.kind == "first" and u == 0)
                    prep = not (t.kind == "last" and u >= 2)
                    for n in range(8):
                        if not (t.kind == "last" and u == 3 and n == 7):
                            nu, nn = (u, n + 1) if n < 7 else ((u + 1) % 4, 0)
                            if nu % 2 == 1 and nn < 2:
                                done = preps_before(t, nu - 1, 4) + 1 if not (t.kind == "last" and nu == 3) \
                                    else preps_before(t, 0, 4) + 1
                                pe.wait_ge(x_free[nn], done)
                            scores(nu, nn)
                        if blk == 0 and n < 6 and prep:
                            project(t, u, n)
                        if n == 1 and has_prev:
                            use_m(t, (u, "R"))
                            turn_recip(unit_no(t, u))
                        if 1 <= n <= 4 and has_prev:
                            if n == 1:
                                before_times_v(t, unit_no(t, u), [turns_before(t, u, 0, i) for i in (0, 1)])
                            times_v(prev, [n - 1] if prev % 2 == 0 else [2 * n - 2, 2 * n - 1])
                        if blk == 1 and n in (2, 4) and prep:
                            half = n // 2 - 1
                            use_m(t, (u, f"V{half}"))
                            project_v(1 - par, half)
                        if u == 0 and n in (2, 4):
                            if n == 2:
                                pe.wait_ge(xf_in, (t.it + 1) * 32)
                                if t.kind == "first":
                                    pe.wait_ge(w1_done, 1)
                            use_m(t, (0, "W1a" if n == 2 else "W1b"))
                            ffn_up(n - 2)
                        if u == 2 and n == 2:
                            use_m(t, (2, "W2"))
                            ffn_down()
                        if n == 6 and has_prev:
                            use_m(t, (u, "O"))
                            project_o(unit_no(t, u), prev // 2, t.it if u == 0 else t.it + 1)
                        turn_step(t, u, n)

            run(pe, body)
            use_m(END, "R")
            turn_recip(unit_no(END, 0))
            before_times_v(END, unit_no(END, 0), [turns_before(END, 0, 0, i) for i in (0, 1)])
            times_v(3, list(range(8)))
            use_m(END, "O")
            project_o(unit_no(END, 0), 1, QUADS)

        @block.scalar
        def _(act):
            copy = lambda dst, src, scale=1.0: nc.scalar.activation(dst, src, ACT.Copy, scale=scale)

            def exponential(t, u, n):
                _, _, _, _, tiles = coords(u, n)
                g = step_no(t, u, n) if t is not None else 0
                act.wait_ge(max_done, g + 1)
                if t is not None and not (t.kind == "first" and u == 0 and n < 2):
                    last_u, last_n = (u, n - 2) if n >= 2 else (u - 1, n + 6)
                    bank = groups(last_u % 4, last_n)[-1][0]
                    act.wait_ge(turn_full[bank], turns_before(t, last_u, last_n, bank) + 1 if last_u >= 0
                                else turns_before(t, 0, 0, bank) + 1
                                - sum(1 for m in range(last_n, 8) for x_ in groups(3, m) if x_[0] == bank))
                i = u % 2
                nc.scalar.activation(prob[n % 2][:, 0:tiles * P], score[n % 2][:, 0:tiles * P], ACT.Exp,
                                     bias=neg_max[:, i, n:n + 1],
                                     accum_out=row_sum[:, i, n:n + 1]).then_inc(exp_done, 1)

            def copy_turned(t, u, n):
                for bank, j0, count in groups(u, n):
                    if bank == 0:
                        par, blk, il, h, _ = coords(u, n)
                        act.wait_ge(turn_full[0], turns_before(t, u, n, 0) + 1)
                        copy(prob_t[blk][:, h, j0:j0 + count, il * P:(il + 1) * P],
                             turned[0][:, 0:count * P].rearrange("p (j q) -> p j q", q=P))\
                            .then_inc(turn_free[0], 1)

            def project_hi(par, s, before):
                bank, what = s % 2, PREP[s]
                tok = slice(what[-1] * BANK, (what[-1] + 1) * BANK)
                act.wait_ge(x_full[bank], before + 1)
                if what[0] == "Q":
                    copy(q_hi[par][:, what[1], tok], x_ps[bank], SCALE).then_inc(x_hi[bank], 1)
                else:
                    copy(k_st[par][0:DH, 0, tok], x_ps[bank][0:DH, :])
                    copy(k_st[par][DH:P, 1, tok], x_ps[bank][DH:P, :]).then_inc(x_hi[bank], 1)

            def split_w(par, count):
                act.wait_ge(set_in[par], count * SET_DMAS)
                copy(w_hi[par][:, :], w_raw[par][:, :]).then_inc(w_hi_done, 1)

            def copy_recip_t(t, key, units_done):
                act.wait_ge(m_full, M_USES.upto(t, key))
                if not (t.kind == "first" and units_done == 1):
                    act.wait_ge(z_done, units_done - 1)
                copy(recip_t[:, :], m_ps[:, :]).then_inc(m_free, 1)

            act.wait_ge(var_ready, 1)
            act.wait_ge(zeroed, 4)
            nc.scalar.activation(rstd[:, :], mean_var[:, :, 1], ACT.Sqrt, bias=eps_sb[:, 0:1])\
              .then_inc(std_ready, 1)
            for n in range(TILES // 4):
                act.wait_ge(xt_full, n + 1)
                if n >= 2:
                    act.wait_ge(xn_out[n - 2], 48)
                st = 3 * (n % 2)
                copy(stage[:, st, :], turned[n % 2][:, :])
                copy(stage[:, st + 1, :].bitcast(F32R), turned[n % 2][:, :]).then_inc(xt_hi_done, 1)
            act.wait_ge(const_in, 64)
            copy(w1_hi[:, :], w1_raw[:, :]).then_inc(w1_hi_done, 1)
            split_w(0, 1)
            split_w(1, 1)
            for s in range(6):
                project_hi(0, s, s // 2)
            act.wait_ge(m_full, 1)
            copy(v[0][:, 0:4, :].rearrange("p j f -> p (j f)"), m_ps[:, :]).then_inc(m_free, 1)
            exponential(None, 0, 0)

            def body(t):
                for u in range(4):
                    par, blk = u // 2, u % 2
                    has_prev = not (t.kind == "first" and u == 0)
                    prep = not (t.kind == "last" and u >= 2)
                    for n in range(8):
                        if blk == 0 and n < 6 and prep:
                            project_hi(1 - par, n, preps_before(t, u, n))
                        if n == 1 and has_prev:
                            copy_recip_t(t, (u, "R"), unit_no(t, u))
                        if u == 0 and n == 2:
                            act.wait_ge(m_full, M_USES.upto(t, (0, "W1a")))
                            for c in (0, 1):
                                last = nc.scalar.activation(h_sb[:, c, :], m_ps[:, c * FT:(c + 1) * FT], ACT.Relu,
                                                            bias=b1_sb[:, c:c + 1])
                            last.then_inc(m_free, 1)
                        if blk == 1 and n == 2 and prep:
                            act.wait_ge(m_full, M_USES.upto(t, (u, "V0")))
                            copy(v[1 - par][:, 0:4, :].rearrange("p j f -> p (j f)"), m_ps[:, :]).then_inc(m_free, 1)
                        if u == 2 and n == 2:
                            act.wait_ge(m_full, M_USES.upto(t, (2, "W2")))
                            if t.kind == "first":
                                act.wait_ge(b2_done, 1)
                            nc.scalar.activation(sig[:, 0, :], m_ps[:, 0:FT], ACT.Exp, bias=b2_sb[:, 1:2],
                                                 scale=-1.0).then_inc(gate_exp, 1)
                        if blk == 1 and n == 5 and t.kind != "last":
                            split_w(0 if u == 1 else 1, t.it + 2)
                        if not (t.kind == "last" and u == 3 and n == 7):
                            if n < 7:
                                exponential(t, u, n + 1)
                            elif u < 3:
                                exponential(t, u + 1, 0)
                            else:
                                exponential(Turn(t.it + 1, "mid"), 0, 0)
                        if n == 0 and t.kind != "first" or n == 0 and u >= 2:
                            act.wait_ge(pv_done, unit_no(t, u) - 1)
                        copy_turned(t, u, n)

            run(act, body)
            copy_recip_t(END, "R", unit_no(END, 0))

        @block.vector
        def _(dve):
            def row_max(t, u, n):
                _, _, _, _, tiles = coords(u, n)
                dve.wait_ge(scored, (step_no(t, u, n) if t is not None else 0) + 1)
                nc.vector.tensor_reduce(out=neg_max[:, u % 2, n:n + 1], in_=score[n % 2][:, 0:tiles * P],
                                        axis=AX_X, op=ALU.max, negate=True).then_inc(max_done, 1)

            def copy_turned(t, u, n):
                for bank, j0, count in groups(u, n):
                    if bank == 1:
                        par, blk, il, h, _ = coords(u, n)
                        dve.wait_ge(turn_full[1], turns_before(t, u, n, 1) + 1)
                        nc.vector.tensor_copy(prob_t[blk][:, h, j0:j0 + count, il * P:(il + 1) * P],
                                              turned[1][:, 0:count * P].rearrange("p (j q) -> p j q", q=P))\
                          .then_inc(turn_free[1], 1)

            def project_lo(par, s, before):
                bank, what = s % 2, PREP[s]
                tok = slice(what[-1] * BANK, (what[-1] + 1) * BANK)
                dve.wait_ge(x_hi[bank], before + 1)
                if what[0] == "Q":
                    nc.vector.scalar_tensor_tensor(
                        out=q_lo[par][:, what[1], tok], in0=x_ps[bank], scalar=SCALE,
                        in1=q_hi[par][:, what[1], tok].bitcast(F32), op0=ALU.mult, op1=ALU.subtract)\
                      .then_inc(x_free[bank], 1)
                else:
                    nc.vector.tensor_tensor(k_st[par][DH:P, 0, tok], x_ps[bank][0:DH, :],
                                            k_st[par][0:DH, 0, tok].bitcast(F32), ALU.subtract)
                    nc.vector.tensor_tensor(k_st[par][0:DH, 1, tok], x_ps[bank][DH:P, :],
                                            k_st[par][DH:P, 1, tok].bitcast(F32), ALU.subtract)\
                      .then_inc(x_free[bank], 1)

            def split_w(par, count):
                dve.wait_ge(w_hi_done, count)
                nc.vector.tensor_tensor(w_lo[par][:, :], w_raw[par][:, :], w_hi[par][:, :].bitcast(F32),
                                        ALU.subtract).then_inc(w_lo_done, 1)

            def reciprocals(t, u):
                done = unit_no(t, u)
                dve.wait_ge(exp_done, step_no(t, u, 0))
                nc.vector.reciprocal(recip[:, :], row_sum[:, (u - 1) % 2, :]).then_inc(recip_chain, 1)
                dve.wait_ge(recip_chain, done)
                nc.vector.tensor_copy(recip_wide[:, :, :], recip[:, :].unsqueeze(2).to_broadcast([P, 8, DH]))\
                  .then_inc(recip_ready, 1)

            def normalise(t, key, done):
                dve.wait_ge(pv_done, done)
                dve.wait_ge(m_free, M_USES.upto(t, key))
                nc.vector.tensor_tensor(z[:, :], z_ps[:, :], recip_t[:, :], ALU.mult).then_inc(z_done, 1)

            def add_output(t, key, tok):
                dve.wait_ge(m_full, M_USES.upto(t, key))
                nc.vector.tensor_tensor(s_t[:, tok], m_ps[:, :], s_t[:, tok], ALU.add).then_inc(m_free, 1)

            for b in range(BATCHES):
                dve.wait_ge(x_in[b], 16)
                for i in range(b * SEQ_TILES, (b + 1) * SEQ_TILES):
                    nc.vector.bn_stats(stats[:, i, :], x_nat[:, i, :]).then_inc(stats_done, 1)
            for i in range(TILES):
                dve.wait_ge(stats_done, TILES if i else TILES)
                last = nc.vector.bn_aggr(mean_var[:, i, :], stats[:, i, :])
            last.then_inc(var_ready, 1)
            dve.wait_ge(std_ready, 1)
            nc.vector.reciprocal(rstd[:, :], rstd[:, :]).then_inc(rstd_ready, 1)
            dve.wait_ge(rstd_ready, 1)

            def normalise_tiles(n):
                for i in range(4 * n, 4 * n + 4):
                    nc.vector.tensor_scalar(x_nat[:, i, :], x_nat[:, i, :], mean_var[:, i, 0:1], rstd[:, i:i + 1],
                                            ALU.subtract, ALU.mult).then_inc(xn_ready, 1)

            normalise_tiles(0)
            normalise_tiles(1)
            for n in range(TILES // 4):
                if n + 2 < TILES // 4:
                    normalise_tiles(n + 2)
                dve.wait_ge(xt_hi_done, n + 1)
                st = 3 * (n % 2)
                nc.vector.tensor_tensor(stage[:, st + 2, :].bitcast(F32R), turned[n % 2][:, :],
                                        stage[:, st + 1, :], ALU.subtract).then_inc(xt_lo_done, 1)
            dve.wait_ge(w1_hi_done, 1)
            nc.vector.tensor_tensor(w1_lo[:, :], w1_raw[:, :], w1_hi[:, :].bitcast(F32), ALU.subtract)\
              .then_inc(w1_done, 1)
            nc.vector.tensor_scalar(b2_sb[:, 1:2], b2_sb[:, 0:1], -1.0, None, ALU.mult).then_inc(b2_done, 1)
            split_w(0, 1)
            split_w(1, 2)
            for s in range(6):
                project_lo(0, s, s // 2)
            dve.wait_ge(m_full, 2)
            nc.vector.tensor_copy(v[0][:, 4:8, :].rearrange("p j f -> p (j f)"), m_ps[:, :]).then_inc(m_free, 1)
            row_max(None, 0, 0)
            for g in range(TILES // 4):
                dve.wait_ge(xn_out[g], 48)
            dve.wait_ge(s_zeroed, 1)

            def body(t):
                for u in range(4):
                    par, blk = u // 2, u % 2
                    has_prev = not (t.kind == "first" and u == 0)
                    prep = not (t.kind == "last" and u >= 2)
                    for n in range(8):
                        if not (t.kind == "last" and u == 3 and n == 7):
                            if n < 7:
                                row_max(t, u, n + 1)
                            elif u < 3:
                                row_max(t, u + 1, 0)
                            else:
                                row_max(Turn(t.it + 1, "mid"), 0, 0)
                        if n == 0 and has_prev:
                            reciprocals(t, u)
                        if n == 5 and has_prev:
                            normalise(t, (u, "R"), unit_no(t, u))
                        if blk == 0 and n < 6 and prep:
                            project_lo(1 - par, n, preps_before(t, u, n))
                        if u == 0 and n == 4:
                            dve.wait_ge(m_full, M_USES.upto(t, (0, "W1b")))
                            for c in (2, 3):
                                last = nc.vector.tensor_scalar(h_sb[:, c, :], m_ps[:, (c - 2) * FT:(c - 1) * FT],
                                                               b1_sb[:, c:c + 1], 0.0, ALU.add, ALU.max)
                            last.then_inc(m_free, 1)
                        if blk == 1 and n == 4 and prep:
                            dve.wait_ge(m_full, M_USES.upto(t, (u, "V1")))
                            nc.vector.tensor_copy(v[1 - par][:, 4:8, :].rearrange("p j f -> p (j f)"), m_ps[:, :])\
                              .then_inc(m_free, 1)
                        if u == 2 and n == 2:
                            dve.wait_ge(gate_exp, t.it + 1)
                            nc.vector.tensor_scalar(sig[:, 1, :], sig[:, 0, :], 1.0, None, ALU.add)\
                              .then_inc(gate_chain, 1)
                            dve.wait_ge(gate_chain, t.it * 2 + 1)
                            nc.vector.reciprocal(sig[:, 0, :], sig[:, 1, :]).then_inc(gate_chain, 1)
                            dve.wait_ge(gate_chain, t.it * 2 + 2)
                            nc.vector.scalar_tensor_tensor(
                                out=g_t[:, bass.ds(t.it * FT, FT)], in0=m_ps[:, 0:FT], scalar=b2_sb[:, 0:1],
                                in1=sig[:, 0, :], op0=ALU.add, op1=ALU.mult).then_inc(m_free, 1)
                        if blk == 1 and n == 5 and t.kind != "last":
                            split_w(0 if u == 1 else 1, t.it * 2 + (3 if u == 1 else 4))
                        if n == 6 and has_prev:
                            quad = t.it if u else t.it - 1
                            add_output(t, (u, "O"),
                                       bass.ds(batch_of(quad) * SEQ + ((u - 1) % 2) * BANK, BANK))
                        copy_turned(t, u, n)

            run(dve, body)
            reciprocals(END, 0)
            normalise(END, "R", unit_no(END, 0))
            add_output(END, "O", bass.ds(TOKENS - BANK, BANK))
            dve.wait_ge(xt_in, 16)
            dve.wait_ge(m_free, M_USES.upto(END, "O"))
            for c in range(BATCHES):
                tok = slice(c * SEQ, (c + 1) * SEQ)
                nc.vector.tensor_tensor(s_t[:, tok], s_t[:, tok], g_t[:, tok], ALU.mult).then_inc(fin_chain, 1)
            for c in range(BATCHES):
                tok = slice(c * SEQ, (c + 1) * SEQ)
                dve.wait_ge(fin_chain, c + 1)
                nc.vector.tensor_tensor(g_t[:, tok], s_t[:, tok], x_t_sb[:, tok], ALU.add).then_inc(fin_ready, 1)


def kernel(L0_attn_x, L0_attn_W_K, L0_attn_W_Q, L0_attn_W_V, L0_attn_W_O, L0_ffn_W1, L0_ffn_b1,
           L0_ffn_W2, L0_ffn_b2):
    import numpy as np
    import concourse.bacc as bacc
    from concourse.bass_utils import run_bass_kernel_spmd

    lay = np.ascontiguousarray
    batches, seq, d = L0_attn_x.shape
    x = lay(np.asarray(L0_attn_x).reshape(batches * seq, d))
    feature_major = lambda w: lay(np.asarray(w).reshape(-1, d).T)
    arrays = {
        "x": x, "x_t": lay(x.T),
        "wq_t": feature_major(L0_attn_W_Q), "wk_t": feature_major(L0_attn_W_K),
        "wv_t": feature_major(L0_attn_W_V), "wo_t": lay(np.asarray(L0_attn_W_O).T),
        "w1": lay(L0_ffn_W1), "b1": lay(L0_ffn_b1), "w2": lay(L0_ffn_W2), "b2": lay(L0_ffn_b2),
    }
    nc = bacc.Bacc("TRN2", target_bir_lowering=False, num_devices=1)
    args = [nc.dram_tensor(name, a.shape, F32, kind="ExternalInput").ap() for name, a in arrays.items()]
    out_t = nc.dram_tensor("out_t", (d, batches * seq), F32, kind="ExternalOutput").ap()
    attention_gated_by_ffn(nc, *args, out_t)
    done = run_bass_kernel_spmd(nc, [arrays], core_ids=[0])
    return lay(done.results[0]["out_t"].T).reshape(batches, seq, d)
```

```python
from contextlib import ExitStack

import concourse.bass as bass
from concourse import mybir
from concourse.alu_op_type import AluOpType as ALU

F32 = mybir.dt.float32
F32R = mybir.dt.float32r
BF16 = mybir.dt.bfloat16
ACT = mybir.ActivationFunctionType
AX_X = mybir.AxisListType.X
AX_XY = mybir.AxisListType.XY

P = 128
BANK = 512
MASKED = -1.0e10
EPS = 1e-5


class Turn:

    def __init__(self, it, kind):
        self.it, self.kind = it, kind


class Tally:

    def __init__(self, lead, first, body, last, tail):
        self.lead, self.first, self.body, self.last, self.tail = lead, first, body, last, tail

    def upto(self, turn, event):
        if turn.kind == "lead":
            return self.lead.index(event) + 1
        if turn.kind == "first":
            return len(self.lead) + self.first.index(event) + 1
        done = len(self.lead) + len(self.first)
        if turn.kind == "tail":
            return (done + (turn.it - 2) * len(self.body) + len(self.last)
                    + self.tail.index(event) + 1)
        events = self.last if turn.kind == "last" else self.body
        return (turn.it - 1) * len(self.body) + (done + events.index(event) + 1)


def attention_gated_by_ffn(nc, x, x_t, wq_t, wk_t, wv_t, wo_t, w1, b1, w2, b2, out_t):
    TOKENS, D = x.shape
    FF = w1.shape[1]
    DH = 64
    SEQ = 1024
    BATCHES = TOKENS // SEQ
    PAIRS = wq_t.shape[1] // P
    QUADS = BATCHES * PAIRS // 2
    PER_BATCH = QUADS // BATCHES
    TILES = TOKENS // P
    SEQ_TILES = SEQ // P
    GROUPS = TOKENS // BANK
    FC = FF // P
    FT = TOKENS // QUADS
    SCALE = 1.0 / 8.0
    assert D == P and DH * 2 == P and SCALE == DH ** -0.5 and FC * FT == 2 * BANK

    FILLERS = {"PE": [
            {0: [("prep", 0)], 1: [("prep", 1)], 2: [("O",)], 3: [("PV", 0, 1)],
             4: [("prep", 2), ("PV", 2), ("R",)], 5: [("PV", 3, 4), ("prep", 3)], 6: [("PV", 5, 6, 7)]},
            {1: [("O",)], 2: [("PV", 0), ("R",)], 3: [("PV", 1)], 4: [("W1", 0)], 5: [("W1", 1)],
             6: [("W2",)], 7: [("PV", 2, 3)]},
            {0: [("prep", 0)], 2: [("prep", 1), ("O",), ("PV", 0)], 3: [("PV", 1)],
             4: [("PV", 2), ("prep", 2), ("R",)], 5: [("PV", 3, 4), ("prep", 3)], 6: [("PV", 5, 6, 7)]},
            {0: [("V", 0)], 1: [("O",)], 3: [("R",), ("PV", 0), ("V", 1)], 4: [("PV", 1)],
             5: [("V", 2)], 7: [("PV", 2), ("V", 3), ("PV", 3)]},
        ],
        "ACT": [
            {1: [("prep", 0)], 2: [("prep", 1)], 4: [("prep", 2), ("R",)], 5: [("prep", 3)]},
            {2: [("R",)], 3: [("split", 0)], 4: [("W1", 0)], 7: [("W2",)]},
            {0: [("prep", 0)], 3: [("prep", 1)], 4: [("prep", 2), ("R",)], 5: [("prep", 3)]},
            {0: [("V", 0)], 3: [("R",)], 5: [("V", 2)], 6: [("split", 1)]},
        ],
        "DVE": [
            {0: [("Z",)], 1: [("N",), ("prep", 0)], 2: [("prep", 1), ("O",)], 5: [("prep", 2)],
             6: [("prep", 3)]},
            {0: [("Z",), ("N",)], 1: [("O",)], 5: [("W1", 1)], 6: [("split", 0)]},
            {0: [("G",), ("Z",)], 1: [("prep", 0)], 2: [("N",), ("O",)], 4: [("prep", 1)],
             5: [("prep", 2)], 6: [("prep", 3)]},
            {0: [("Z",), ("N",)], 1: [("O",)], 4: [("V", 1)], 6: [("split", 1)], 7: [("V", 3)]},
        ],
    }
    OF_BEFORE = {"N": 1, "R": 1, "PV": 1, "Z": 2, "O": 2}
    TURN_X = {n: ("X", n + 1) for n in range(1, GROUPS - 1)}
    PREP = [("K", 0), ("Q", 0), ("K", 1), ("Q", 1)]

    def fillers(engine, t, u, n):
        found = []
        for f in FILLERS[engine][u].get(n, []):
            if t.kind == "first" and OF_BEFORE.get(f[0], 0) > u:
                continue
            if t.kind == "last" and (f[0] in ("V", "split") or (f[0] == "prep" and u == 2)):
                continue
            found.append(f)
        if t.kind == "first" and u == 0 and n in TURN_X:
            found.append(TURN_X[n])
        return found

    def m_uses(kind):
        return [(u,) + f for u in range(4) for n in range(8) for f in fillers("PE", Turn(0, kind), u, n)
                if f[0] in ("R", "O", "W1", "W2", "V", "X")]

    M_USES = Tally([("V", 0), ("V", 2)], m_uses("first"), m_uses("mid"), m_uses("last"),
                   ["O before", "R", "O"])

    with ExitStack() as ctx:
        def sb(name, shape, dt=F32):
            return ctx.enter_context(nc.sbuf_tensor(name, shape, dt))

        def psum(name, shape):
            return ctx.enter_context(nc.psum_tensor(name, shape, F32))

        def sem(name):
            return ctx.enter_context(nc.semaphore(name))

        xn_hi_dram = nc.dram_tensor("xn_hi", [P, TOKENS], F32, kind="Internal").ap()
        xn_lo_dram = nc.dram_tensor("xn_lo", [P, TOKENS], F32, kind="Internal").ap()

        xh = sb("xh", [P, SEQ], F32R)
        xl = sb("xl", [P, SEQ], F32R)
        W_COLS = [4 * P, 2 * P]
        w_raw = [sb(f"w_raw{i}", [P, W_COLS[i]]) for i in (0, 1)]
        w_hi = [sb(f"w_hi{i}", [P, W_COLS[i]], F32R) for i in (0, 1)]
        w_lo = [sb(f"w_lo{i}", [P, W_COLS[i]], F32R) for i in (0, 1)]
        wo = [sb(f"wo{i}", [P, P]) for i in (0, 1)]
        q_hi = [sb(f"q_hi{i}", [P, 2, SEQ], F32R) for i in (0, 1)]
        q_lo = [sb(f"q_lo{i}", [P, 2, SEQ], F32R) for i in (0, 1)]
        k_st = [sb(f"k_st{i}", [P, 2, SEQ], F32R) for i in (0, 1)]
        v_quad = sb("v_quad", [P, 2, SEQ_TILES, P])
        v_pair1 = sb("v_pair1", [P, SEQ_TILES, P])
        v = [v_quad[:, 0], v_pair1[:, :, :]]
        prob = [sb(f"prob{i}", [P, SEQ]) for i in range(4)]
        prob_t = [sb("prob_t0", [P, 2, 4, BANK]), sb("prob_t1", [P, 2, 8, BANK])]
        neg_max = sb("neg_max", [P, 2, 8])
        row_sum = sb("row_sum", [P, 2, 8])
        recip = sb("recip", [P, 8])
        recip_wide = sb("recip_wide", [P, 8, DH])
        recip_t = sb("recip_t", [P, BANK])
        z = sb("z", [P, BANK])
        s_t = sb("s_t", [P, TOKENS])
        g_t = sb("g_t", [P, TOKENS])
        x_t_sb = sb("x_t_sb", [P, SEQ])
        w1_raw = sb("w1_raw", [P, FF])
        w1_hi = sb("w1_hi", [P, FF], F32R)
        w1_lo = sb("w1_lo", [P, FF], F32R)
        w2_sb = sb("w2_sb", [P, FC, P])
        b1_sb = sb("b1_sb", [P, FC])
        b2_sb = sb("b2_sb", [P, 2])
        xf_hi = sb("xf_hi", [P, FT], F32R)
        xf_lo = sb("xf_lo", [P, FT], F32R)
        h_sb = sb("h_sb", [P, FC, FT])
        sig = sb("sig", [P, 2, FT])
        ident = sb("ident", [P, P])
        ident_b = sb("ident_b", [P, P], BF16)
        mask_b = sb("mask_b", [P, P], BF16)
        stats = sb("stats", [P, TILES, 6])
        mean_var = sb("mean_var", [P, TILES, 2])
        rstd = sb("rstd", [P, TILES])
        eps_sb = sb("eps_sb", [P, 1])
        unused = sb("unused", [P, 1])
        x_nat = prob_t[1][:, :, :, :].rearrange("p h j q -> p (h j q)")[:, 0:TOKENS].rearrange(
            "p (t d) -> p t d", d=D)

        score = [psum(f"score{i}", [P, 2 * BANK]) for i in (0, 1)]
        turned = [psum(f"turned{i}", [P, BANK]) for i in (0, 1)]
        z_ps = psum("z_ps", [P, BANK])
        m_ps = psum("m_ps", [P, BANK])
        x_ps = [score[i][:, BANK:2 * BANK] for i in (0, 1)]

        x_in = [sem(f"x_in{b}") for b in range(BATCHES)]
        ffn_in = sem("ffn_in")
        zeroed = sem("zeroed")
        const_ready = sem("const_ready")
        s_zeroed = [sem(f"s_zeroed{i}") for i in (0, 1)]
        stats_done = sem("stats_done")
        var_ready = sem("var_ready")
        std_ready = sem("std_ready")
        rstd_ready = sem("rstd_ready")
        xn_ready = [sem(f"xn_ready{i}") for i in (0, 1)]
        xt_full = sem("xt_full")
        xt_hi = sem("xt_hi")
        xt_lo = sem("xt_lo")
        xn_out = sem("xn_out")
        xn_rest_out = sem("xn_rest_out")
        w1_hi_done = sem("w1_hi_done")
        w1_done = sem("w1_done")
        b2_done = sem("b2_done")
        xc_in = sem("xc_in")
        w_in = [sem(f"w_in{i}") for i in (0, 1)]
        wo_in = [sem(f"wo_in{i}") for i in (0, 1)]
        xf_in = sem("xf_in")
        w_hi_done = sem("w_hi_done")
        w_lo_done = sem("w_lo_done")
        x_full = [sem(f"x_full{i}") for i in (0, 1)]
        x_hi = [sem(f"x_hi{i}") for i in (0, 1)]
        x_free = [sem(f"x_free{i}") for i in (0, 1)]
        q_twice = [[sem(f"q_twice{i}{blk}") for blk in (0, 1)] for i in (0, 1)]
        scored = sem("scored")
        max_done = sem("max_done")
        exp_done = sem("exp_done")
        turn_full = [sem(f"turn_full{i}") for i in (0, 1)]
        turn_free = [sem(f"turn_free{i}") for i in (0, 1)]
        recip_chain = sem("recip_chain")
        recip_ready = sem("recip_ready")
        v_copied = sem("v_copied")
        pv_done = sem("pv_done")
        z_done = sem("z_done")
        v_full = sem("v_full")
        v_free = sem("v_free")
        m_full = sem("m_full")
        m_free = sem("m_free")
        gate_exp = sem("gate_exp")
        gate_chain = sem("gate_chain")
        xt_in = sem("xt_in")
        fin_pool = sem("fin_pool")
        fin_chain = sem("fin_chain")
        fin_ready = sem("fin_ready")
        out_done = sem("out_done")
        last_out = sem("last_out")

        block = ctx.enter_context(nc.Block())

        def coords(u, n):
            par, blk, il, h = u // 2, u % 2, n // 2, n % 2
            return par, blk, il, h, 4 * blk + il + 1

        def groups(u, n):
            _, blk, _, _, tiles = coords(u, n)
            if blk == 0:
                return [(n % 2, 0, tiles)]
            return [(0, 0, 4), (1, 4, tiles - 4)]

        def pieces(tiles):
            keys = tiles * P
            if tiles == 5:
                return [(0, 0, keys // 2), (BANK, keys // 2, keys // 2)]
            return [(k, k, max(min(keys - k, BANK), 2 * P)) for k in range(0, keys, BANK)]

        def scores_and_probs(n, tiles):
            if tiles == 5:
                half = tiles * P // 2
                return (score[n % 2][:, :].rearrange("p (b c) -> p b c", b=2)[:, :, 0:half],
                        prob[n % 4][:, 0:tiles * P].rearrange("p (b c) -> p b c", b=2))
            return score[n % 2][:, 0:tiles * P], prob[n % 4][:, 0:tiles * P]

        TURNS_OF = [[sum(1 for n in range(8) for g in groups(u, n) if g[0] == i) for u in range(4)]
                    for i in (0, 1)]
        TURNS = sum(TURNS_OF[0])
        assert TURNS == sum(TURNS_OF[1])

        def turns_before(t, u, n, bank):
            k = sum(TURNS_OF[bank][:u]) + sum(1 for m in range(n) for g in groups(u, m) if g[0] == bank)
            return t.it * TURNS + k

        def back(t, u, n, steps):
            k = u * 8 + n - steps
            if k >= 0:
                return t, k // 8, k % 8
            if t.kind == "first":
                return None
            return Turn(t.it - 1, "mid"), (k + 32) // 8, (k + 32) % 8

        def ahead(t, u, n):
            k = u * 8 + n + 1
            if k < 32:
                return t, k // 8, k % 8
            return None if t.kind == "last" else (Turn(t.it + 1, "mid"), 0, 0)

        def preps_before(t, u, s):
            return t.it * 4 + (2 + (u // 2) * 2 + s // 2)

        def step_no(t, u, n):
            return t.it * 32 + (u * 8 + n)

        def unit_no(t, u):
            return t.it * 4 + u

        def batch_of(quad):
            return quad // PER_BATCH

        def pair_of(quad, par):
            return (quad % PER_BATCH) * 2 + par

        def run(engine, body):
            body(Turn(0, "first"))
            with engine.Fori(1, QUADS - 1) as it:
                body(Turn(it, "mid"))
            body(Turn(QUADS - 1, "last"))

        LEAD = Turn(0, "lead")
        END = Turn(QUADS, "tail")

        @block.sync
        def _(sp):
            xv = x.rearrange("(t p) d -> p t d", p=P)

            def load_w(par, quad):
                col = bass.ds(pair_of(quad, par) * P, P)
                sp.dma_start(w_raw[par][:, 0:P], wq_t[:, col]).then_inc(w_in[par], 16)
                sp.dma_start(w_raw[par][:, P:2 * P], wk_t[:, col]).then_inc(w_in[par], 16)
                if par == 0:
                    sp.dma_start(w_raw[0][:, 2 * P:4 * P], wv_t[:, bass.ds(pair_of(quad, 0) * P, 2 * P)])\
                      .then_inc(w_in[0], 16)

            def load_x(quad):
                tok = bass.ds(batch_of(quad) * SEQ, SEQ)
                sp.dma_start(xh[:, :].bitcast(F32), xn_hi_dram[:, tok]).then_inc(xc_in, 16)
                sp.dma_start(xl[:, :].bitcast(F32), xn_lo_dram[:, tok]).then_inc(xc_in, 16)

            def load_wo(par, quad):
                sp.dma_start(wo[par][:, :], wo_t[bass.ds(pair_of(quad, par) * P, P), :])\
                  .then_inc(wo_in[par], 16)

            def load_xf(quad):
                tok = bass.ds(quad * FT, FT)
                sp.dma_start(xf_hi[:, :].bitcast(F32), xn_hi_dram[:, tok]).then_inc(xf_in, 16)
                sp.dma_start(xf_lo[:, :].bitcast(F32), xn_lo_dram[:, tok]).then_inc(xf_in, 16)

            def double_q(par, blk, uses):
                tok = slice(blk * BANK, (blk + 1) * BANK)
                for part, stands in ((q_hi, x_hi), (q_lo, x_free)):
                    sp.wait_ge(stands[1], uses)
                    for h in (0, 1):
                        here, there = slice(h * DH, (h + 1) * DH), slice((1 - h) * DH, (2 - h) * DH)
                        sp.dma_start(part[par][there, h, tok].bitcast(F32), part[par][here, h, tok].bitcast(F32))\
                          .then_inc(q_twice[par][blk], 16)

            def load_tiles(b):
                ts = slice(b * SEQ_TILES, (b + 1) * SEQ_TILES)
                sp.dma_start(x_nat[:, ts, :], xv[:, ts, :]).then_inc(x_in[b], 16)

            load_tiles(0)
            load_w(0, 0)
            for b in range(1, BATCHES):
                load_tiles(b)
            load_w(1, 0)
            sp.dma_start(w1_raw[:, :], w1).then_inc(ffn_in, 16)
            sp.dma_start(w2_sb[:, :, :], w2.rearrange("(c p) d -> p c d", p=P)).then_inc(ffn_in, 16)
            with nc.allow_non_contiguous_dma(reason="two small vectors"):
                sp.dma_start(b1_sb[:, :], b1.rearrange("(c p) -> p c", p=P)).then_inc(ffn_in, 16)
                sp.dma_start(b2_sb[:, 0:1], b2.rearrange("(p a) -> p a", a=1)).then_inc(ffn_in, 16)
            load_wo(0, 0)
            load_wo(1, 0)
            sp.wait_ge(xt_lo, 2)
            sp.dma_start(xn_hi_dram[:, 0:SEQ], xh[:, :].bitcast(F32)).then_inc(xn_out, 16)
            sp.dma_start(xn_lo_dram[:, 0:SEQ], xl[:, :].bitcast(F32)).then_inc(xn_out, 16)
            for blk in (0, 1):
                double_q(0, blk, blk + 1)
            sp.wait_ge(xn_out, 32)
            load_xf(0)

            def body(t):
                if t.kind == "mid":
                    sp.wait_ge(m_full, M_USES.upto(t, (0, "R")) - 1)
                if t.kind == "first":
                    sp.wait_ge(m_full, len(M_USES.lead))
                    sp.wait_ge(v_full, 2)
                if t.kind != "last":
                    load_w(0, t.it + 1)
                for blk in (0, 1):
                    double_q(1, blk, preps_before(t, 0, 2 * blk + 1) + 1)
                if t.kind != "last":
                    sp.wait_ge(x_full[1], preps_before(t, 0, 3) + 1)
                    if t.kind == "first":
                        sp.wait_ge(xn_rest_out, 32 * (GROUPS - 2))
                    load_x(t.it + 1)
                    load_w(1, t.it + 1)
                if t.kind != "first":
                    sp.wait_ge(m_full, M_USES.upto(t, (1, "O")))
                    load_wo(1, t.it)
                if t.kind != "last":
                    sp.wait_ge(m_full, M_USES.upto(t, (1, "W1", 1)))
                    load_xf(t.it + 1)
                    for blk in (0, 1):
                        double_q(0, blk, preps_before(t, 2, 2 * blk + 1) + 1)
                    sp.wait_ge(m_full, M_USES.upto(t, (3, "O")))
                    load_wo(0, t.it + 1)

            run(sp, body)
            sp.wait_ge(fin_ready, 1)
            sp.dma_start(out_t[:, TOKENS - BANK:TOKENS], g_t[:, TOKENS - BANK:TOKENS]).then_inc(last_out, 16)
            sp.wait_ge(last_out, 16)

        @block.gpsimd
        def _(pool):
            nc.gpsimd.memset(ident[:, :], 0.0).then_inc(zeroed, 1)
            nc.gpsimd.memset(ident_b[:, :], 0.0).then_inc(zeroed, 1)
            nc.gpsimd.memset(mask_b[:, :], 0.0).then_inc(zeroed, 1)
            nc.gpsimd.memset(eps_sb[:, :], EPS).then_inc(zeroed, 1)
            pool.wait_ge(zeroed, 4)
            for m in (ident, ident_b):
                nc.gpsimd.affine_select(out=m[:, :], in_=m[:, :], compare_op=ALU.not_equal, fill=1.0,
                                        base=0, pattern=[[-1, P]], channel_multiplier=1)\
                  .then_inc(const_ready, 1)
            nc.gpsimd.affine_select(out=mask_b[:, :], in_=mask_b[:, :], compare_op=ALU.is_ge,
                                    fill=MASKED * SCALE, base=0, pattern=[[-1, P]],
                                    channel_multiplier=1).then_inc(const_ready, 1)
            nc.gpsimd.memset(s_t[:, 0:SEQ], 0.0).then_inc(s_zeroed[0], 1)
            pool.wait_ge(rstd_ready, 2)
            for i in range(SEQ_TILES, TILES):
                nc.gpsimd.tensor_scalar(x_nat[:, i, :], x_nat[:, i, :], mean_var[:, i, 0:1], rstd[:, i:i + 1],
                                        ALU.subtract, ALU.mult).then_inc(xn_ready[1], 1)

            def copy_v(quad):
                nc.gpsimd.tensor_copy(v_pair1[:, :, :], v_quad[:, 1]).then_inc(v_copied, 1)

            pool.wait_ge(m_free, len(M_USES.lead))
            pool.wait_ge(v_free, 2)
            copy_v(0)
            for n in range(2, GROUPS):
                pool.wait_ge(m_free, M_USES.upto(Turn(0, "first"), (0, "X", n)))
                tok = slice(n * BANK, (n + 1) * BANK)
                pool.dma_start(xn_hi_dram[:, tok], g_t[:, tok]).then_inc(xn_rest_out, 16)
                pool.dma_start(xn_lo_dram[:, tok], s_t[:, tok]).then_inc(xn_rest_out, 16)
            pool.wait_ge(xn_rest_out, 32 * (GROUPS - 2))
            nc.gpsimd.memset(s_t[:, SEQ:TOKENS], 0.0).then_inc(s_zeroed[1], 1)

            def finish(b, tok, part, count):
                pool.wait_ge(xt_in, (b + 1) * 16)
                nc.gpsimd.tensor_tensor(s_t[:, tok], s_t[:, tok], g_t[:, tok], ALU.mult).then_inc(fin_pool, 1)
                pool.wait_ge(fin_pool, count * 2 + 1)
                nc.gpsimd.tensor_tensor(g_t[:, tok], s_t[:, tok], x_t_sb[:, part], ALU.add).then_inc(fin_pool, 1)
                pool.wait_ge(fin_pool, count * 2 + 2)
                pool.dma_start(out_t[:, tok], g_t[:, tok]).then_inc(out_done, 16)

            def load_x_t(b):
                pool.dma_start(x_t_sb[:, :], x_t[:, b * SEQ:(b + 1) * SEQ]).then_inc(xt_in, 16)

            load_x_t(0)
            for quad in range(1, QUADS):
                t = Turn(quad, "mid")
                pool.wait_ge(pv_done, quad * 4)
                pool.wait_ge(m_free, M_USES.upto(t, (0, "R")) - 1)
                copy_v(quad)
                if quad % PER_BATCH == 0:
                    b = quad // PER_BATCH - 1
                    pool.wait_ge(m_free, M_USES.upto(t, (1, "O")))
                    finish(b, slice(b * SEQ, (b + 1) * SEQ), slice(0, SEQ), b)
                    load_x_t(b + 1)
            pool.wait_ge(m_free, M_USES.upto(END, "O before"))
            finish(BATCHES - 1, slice(TOKENS - SEQ, TOKENS - BANK), slice(0, BANK), BATCHES - 1)
            pool.wait_ge(out_done, 16 * BATCHES)

        @block.tensor
        def _(pe):
            mm = nc.tensor.matmul

            def three_passes(out, hi_lo, cols, hi, lo):
                w_h, w_l = hi_lo
                mm(out, w_h[:, cols], hi, start=True, stop=False)
                mm(out, w_h[:, cols], lo, start=False, stop=False)
                return mm(out, w_l[:, cols], hi, start=False, stop=True)

            def scores(t, u, n):
                par, blk, il, h, tiles = coords(u, n)
                if n == 0:
                    pe.wait_ge(q_twice[par][blk], (t.it + 1) * 64)
                if back(t, u, n, 2):
                    pe.wait_ge(exp_done, step_no(t, u, n) - 1)
                q0 = (4 * blk + il) * P
                cut = pieces(tiles)
                for col, key, width in cut:
                    dst = score[n % 2][:, col:col + width]
                    keys = k_st[par][:, h, key:key + width]
                    mm(dst, q_hi[par][:, h, q0:q0 + P], keys, start=True, stop=False)
                    mm(dst, q_lo[par][:, h, q0:q0 + P], keys, start=False, stop=(col, key, width) != cut[-1])
                diagonal = cut[-1][0] + (tiles - 1) * P - cut[-1][1]
                mm(score[n % 2][:, diagonal:diagonal + P], ident_b[:, :], mask_b[:, :], start=False, stop=True)\
                    .then_inc(scored, 1)

            def turn_step(t, u, n):
                pe.wait_ge(exp_done, step_no(t, u, n) + 1)
                for bank, j0, count in groups(u, n):
                    before = turns_before(t, u, n, bank)
                    if not (t.kind == "first" and before == 0):
                        pe.wait_ge(turn_free[bank], before)
                    for j in range(count):
                        last = nc.tensor.transpose(turned[bank][:, j * P:(j + 1) * P],
                                                   prob[n % 4][:, (j0 + j) * P:(j0 + j + 1) * P],
                                                   ident[:, :])
                    last.then_inc(turn_full[bank], 1)

            def turn_tiles(dst, tile0):
                for i in range(4):
                    last = nc.tensor.transpose(dst[:, i * P:(i + 1) * P], x_nat[:, tile0 + i, :], ident[:, :])
                return last

            def project(par, s):
                bank, (what, blk) = s % 2, PREP[s]
                tok = slice(blk * BANK, (blk + 1) * BANK)
                cols = slice(0, P) if what == "Q" else slice(P, 2 * P)
                three_passes(x_ps[bank], (w_hi[par], w_lo[par]), cols, xh[:, tok], xl[:, tok])\
                    .then_inc(x_full[bank], 1)

            def project_v(k, bank=m_ps):
                wv_cols = slice(2 * P, 4 * P)
                for i in (0, 1):
                    tok = slice((2 * k + i) * P, (2 * k + i + 1) * P)
                    dst = bank[:, i * 2 * P:(i + 1) * 2 * P]
                    mm(dst, xh[:, tok], w_hi[0][:, wv_cols], start=True, stop=False)
                    mm(dst, xh[:, tok], w_lo[0][:, wv_cols], start=False, stop=False)
                    last = mm(dst, xl[:, tok], w_hi[0][:, wv_cols], start=False, stop=True)
                last.then_inc(m_full if bank is m_ps else v_full, 1)

            def ffn_up(half):
                for i in (0, 1):
                    c = 2 * half + i
                    last = three_passes(m_ps[:, i * FT:(i + 1) * FT], (w1_hi, w1_lo),
                                        slice(c * P, (c + 1) * P), xf_hi[:, :], xf_lo[:, :])
                last.then_inc(m_full, 1)

            def ffn_down():
                for c in range(FC):
                    last = mm(m_ps[:, 0:FT], w2_sb[:, c, :], h_sb[:, c, :], start=(c == 0), stop=(c == FC - 1))
                last.then_inc(m_full, 1)

            def turn_recip(units_done):
                pe.wait_ge(recip_ready, units_done)
                for il in range(4):
                    last = nc.tensor.transpose(m_ps[:, il * P:(il + 1) * P],
                                               recip_wide[:, 2 * il:2 * il + 2, :].rearrange("p h c -> p (h c)"),
                                               ident[:, :])
                last.then_inc(m_full, 1)

            def times_v(t, u, units_done, js):
                par, blk = ((u - 1) % 4) // 2, (u - 1) % 2
                count = 4 * (blk + 1)
                if js[0] == 0:
                    for i in (0, 1):
                        pe.wait_ge(turn_free[i], turns_before(t, u, 0, i))
                    if t.kind == "first" and units_done == 1:
                        pe.wait_ge(v_free, 2)
                    else:
                        pe.wait_ge(z_done, units_done - 1)
                    if par == 1 and blk == 0:
                        pe.wait_ge(v_copied, t.it + 1)
                for j in js:
                    q0 = max(0, j - 4 * blk) * P
                    for h in (0, 1):
                        last = mm(z_ps[h * DH:(h + 1) * DH, q0:BANK], v[par][:, j, h * DH:(h + 1) * DH],
                                  prob_t[blk][:, h, j, q0:BANK], start=(j == 0), stop=(j == count - 1))
                if js[-1] == count - 1:
                    last.then_inc(pv_done, 1)

            def project_o(units_done, par, wo_count):
                pe.wait_ge(wo_in[par], wo_count * 16)
                pe.wait_ge(z_done, units_done)
                mm(m_ps[:, :], wo[par][:, :], z[:, :], start=True, stop=True).then_inc(m_full, 1)

            pe.wait_ge(const_ready, 3)
            for n in (0, 1):
                pe.wait_ge(xn_ready[0], 4 * (n + 1))
                turn_tiles(turned[n], 4 * n).then_inc(xt_full, 1)
            pe.wait_ge(w_lo_done, 1)
            for blk in (0, 1):
                pe.wait_ge(xt_lo, blk + 1)
                for s in (2 * blk, 2 * blk + 1):
                    if blk:
                        pe.wait_ge(x_free[s % 2], 1)
                    project(0, s)
                if blk:
                    pe.wait_ge(m_free, 1)
                project_v(2 * blk)
                if blk:
                    pe.wait_ge(v_free, 1)
                project_v(2 * blk + 1, z_ps)
            for i in (0, 1):
                pe.wait_ge(x_free[i], 2)
            scores(Turn(0, "first"), 0, 0)

            def body(t):
                for u in range(4):
                    par, blk = u // 2, u % 2
                    for n in range(8):
                        if nxt := ahead(t, u, n):
                            if nxt[1] % 2 == 1 and nxt[2] < 2:
                                of = 0 if t.kind == "last" else nxt[1] - 1
                                pe.wait_ge(x_free[nxt[2]], preps_before(t, of, 2) + 1)
                            scores(*nxt)
                        for f in fillers("PE", t, u, n):
                            if f[0] in ("R", "O", "W1", "W2", "V", "X"):
                                pe.wait_ge(m_free, M_USES.upto(t, (u,) + f) - 1)
                            if f[0] == "prep":
                                if f[1] == 0:
                                    pe.wait_ge(w_lo_done, t.it * 2 + (2 if u == 0 else 3))
                                    if u == 2:
                                        pe.wait_ge(xc_in, (t.it + 1) * 32)
                                pe.wait_ge(x_free[f[1] % 2], preps_before(t, u, f[1]))
                                project(1 - par, f[1])
                            if f[0] == "R":
                                turn_recip(unit_no(t, u))
                            if f[0] == "PV":
                                times_v(t, u, unit_no(t, u), f[1:])
                            if f[0] == "O":
                                project_o(unit_no(t, u) - 1, ((u - 2) % 4) // 2, t.it if u < 2 else t.it + 1)
                            if f[0] == "W1":
                                if f[1] == 0:
                                    pe.wait_ge(xf_in, (t.it + 1) * 32)
                                    if t.kind == "first":
                                        pe.wait_ge(w1_done, 1)
                                ffn_up(f[1])
                            if f[0] == "W2":
                                ffn_down()
                            if f[0] == "V":
                                project_v(f[1])
                            if f[0] == "X":
                                pe.wait_ge(xn_ready[1], 4 * (f[1] - 1))
                                turn_tiles(m_ps, 4 * f[1]).then_inc(m_full, 1)
                        if old := back(t, u, n, 1):
                            turn_step(*old)

            run(pe, body)
            turn_step(Turn(QUADS - 1, "last"), 3, 7)
            times_v(END, 0, unit_no(END, 0), (0, 1, 2))
            pe.wait_ge(m_free, M_USES.upto(END, "O before") - 1)
            project_o(unit_no(END, 0) - 1, 1, QUADS)
            times_v(END, 0, unit_no(END, 0), (3, 4))
            pe.wait_ge(m_free, M_USES.upto(END, "R") - 1)
            turn_recip(unit_no(END, 0))
            times_v(END, 0, unit_no(END, 0), (5, 6, 7))
            pe.wait_ge(m_free, M_USES.upto(END, "O") - 1)
            project_o(unit_no(END, 0), 1, QUADS)

        @block.scalar
        def _(act):
            copy = lambda dst, src, scale=1.0: nc.scalar.activation(dst, src, ACT.Copy, scale=scale)

            def exponential(t, u, n):
                _, _, _, _, tiles = coords(u, n)
                act.wait_ge(max_done, step_no(t, u, n) + 1)
                if old := back(t, u, n, 4):
                    bank = groups(*old[1:])[-1][0]
                    act.wait_ge(turn_full[bank], turns_before(*old, bank) + 1)
                i = u % 2
                scores, probs = scores_and_probs(n, tiles)
                nc.scalar.activation(probs, scores, ACT.Exp,
                                     bias=neg_max[:, i, n:n + 1],
                                     accum_out=row_sum[:, i, n:n + 1]).then_inc(exp_done, 1)

            def copy_turned(t, u, n):
                for bank, j0, count in groups(u, n):
                    if bank == 0:
                        _, blk, il, h, _ = coords(u, n)
                        if n == 0 and not (t.kind == "first" and u < 2):
                            act.wait_ge(pv_done, unit_no(t, u) - 1)
                        act.wait_ge(turn_full[0], turns_before(t, u, n, 0) + 1)
                        copy(prob_t[blk][:, h, j0:j0 + count, il * P:(il + 1) * P],
                             turned[0][:, 0:count * P].rearrange("p (j q) -> p j q", q=P))\
                            .then_inc(turn_free[0], 1)

            def project_hi(par, s, before):
                bank, (what, blk) = s % 2, PREP[s]
                tok = slice(blk * BANK, (blk + 1) * BANK)
                act.wait_ge(x_full[bank], before + 1)
                dst, scale = (q_hi, SCALE) if what == "Q" else (k_st, 1.0)
                copy(dst[par][0:DH, 0, tok], x_ps[bank][0:DH, :], scale)
                copy(dst[par][DH:P, 1, tok], x_ps[bank][DH:P, :], scale).then_inc(x_hi[bank], 1)

            def split_w(par, count):
                act.wait_ge(w_in[par], count * 16 * (W_COLS[par] // (2 * P) + 1))
                copy(w_hi[par][:, :], w_raw[par][:, :]).then_inc(w_hi_done, 1)

            def copy_recip_t(t, key, units_done):
                act.wait_ge(m_full, M_USES.upto(t, key))
                if not (t.kind == "first" and units_done == 1):
                    act.wait_ge(z_done, units_done - 1)
                copy(recip_t[:, :], m_ps[:, :]).then_inc(m_free, 1)

            def copy_v(t, k, uses):
                act.wait_ge(m_full, uses)
                if t.kind != "lead":
                    act.wait_ge(v_copied, t.it + 1)
                copy(v_quad[:, :, 2 * k:2 * k + 2, :],
                     m_ps[:, :].rearrange("p (j r f) -> p r j f", j=2, r=2)).then_inc(m_free, 1)

            act.wait_ge(zeroed, 4)
            nc.scalar.activation(unused[:, :], eps_sb[:, 0:1], ACT.Sqrt)
            split_w(0, 1)
            act.wait_ge(var_ready, 1)
            nc.scalar.activation(rstd[:, 0:SEQ_TILES], mean_var[:, 0:SEQ_TILES, 1], ACT.Sqrt,
                                 bias=eps_sb[:, 0:1]).then_inc(std_ready, 1)
            for n in (0, 1):
                act.wait_ge(xt_full, n + 1)
                copy(xh[:, n * BANK:(n + 1) * BANK], turned[n][:, :]).then_inc(xt_hi, 1)
            for blk in (0, 1):
                for s in (2 * blk, 2 * blk + 1):
                    project_hi(0, s, blk)
                copy_v(LEAD, 2 * blk, blk + 1)
            act.wait_ge(var_ready, 2)
            nc.scalar.activation(rstd[:, SEQ_TILES:TILES], mean_var[:, SEQ_TILES:TILES, 1], ACT.Sqrt,
                                 bias=eps_sb[:, 0:1]).then_inc(std_ready, 1)
            split_w(1, 1)
            act.wait_ge(ffn_in, 64)
            copy(w1_hi[:, :], w1_raw[:, :]).then_inc(w1_hi_done, 1)
            exponential(Turn(0, "first"), 0, 0)

            def body(t):
                for u in range(4):
                    par, blk = u // 2, u % 2
                    for n in range(8):
                        for f in fillers("ACT", t, u, n):
                            if f[0] == "prep":
                                project_hi(1 - par, f[1], preps_before(t, u, f[1]))
                            if f[0] == "R":
                                copy_recip_t(t, (u, "R"), unit_no(t, u))
                            if f == ("W1", 0):
                                act.wait_ge(m_full, M_USES.upto(t, (u,) + f))
                                for c in (0, 1):
                                    last = nc.scalar.activation(h_sb[:, c, :], m_ps[:, c * FT:(c + 1) * FT],
                                                                ACT.Relu, bias=b1_sb[:, c:c + 1])
                                last.then_inc(m_free, 1)
                            if f[0] == "V" and f[1] % 2 == 0:
                                copy_v(t, f[1], M_USES.upto(t, (u,) + f))
                            if f[0] == "W2":
                                act.wait_ge(m_full, M_USES.upto(t, (u,) + f))
                                if t.kind == "first":
                                    act.wait_ge(b2_done, 1)
                                nc.scalar.activation(sig[:, 0, :], m_ps[:, 0:FT], ACT.Exp, bias=b2_sb[:, 1:2],
                                                     scale=-1.0).then_inc(gate_exp, 1)
                            if f[0] == "split":
                                split_w(f[1], t.it + 2)
                            if f[0] == "X":
                                act.wait_ge(m_full, M_USES.upto(t, (u,) + f))
                                copy(g_t[:, f[1] * BANK:(f[1] + 1) * BANK].bitcast(F32R), m_ps[:, :])\
                                    .then_inc(xt_hi, 1)
                        if old := back(t, u, n, 1):
                            copy_turned(*old)
                        if nxt := ahead(t, u, n):
                            exponential(*nxt)

            run(act, body)
            copy_turned(Turn(QUADS - 1, "last"), 3, 7)
            copy_recip_t(END, "R", unit_no(END, 0))

        @block.vector
        def _(dve):
            def row_max(t, u, n):
                _, _, _, _, tiles = coords(u, n)
                dve.wait_ge(scored, step_no(t, u, n) + 1)
                scores, _ = scores_and_probs(n, tiles)
                nc.vector.tensor_reduce(out=neg_max[:, u % 2, n:n + 1], in_=scores,
                                        axis=AX_XY if tiles == 5 else AX_X, op=ALU.max, negate=True)\
                    .then_inc(max_done, 1)

            def copy_turned(t, u, n):
                for bank, j0, count in groups(u, n):
                    if bank == 1:
                        _, blk, il, h, _ = coords(u, n)
                        dve.wait_ge(turn_full[1], turns_before(t, u, n, 1) + 1)
                        nc.vector.tensor_copy(prob_t[blk][:, h, j0:j0 + count, il * P:(il + 1) * P],
                                              turned[1][:, 0:count * P].rearrange("p (j q) -> p j q", q=P))\
                          .then_inc(turn_free[1], 1)

            def project_lo(par, s, before):
                bank, (what, blk) = s % 2, PREP[s]
                tok = slice(blk * BANK, (blk + 1) * BANK)
                dve.wait_ge(x_hi[bank], before + 1)
                for h in (0, 1):
                    here, there = slice(h * DH, (h + 1) * DH), slice((1 - h) * DH, (2 - h) * DH)
                    if what == "Q":
                        last = nc.vector.scalar_tensor_tensor(
                            out=q_lo[par][here, h, tok], in0=x_ps[bank][here, :], scalar=SCALE,
                            in1=q_hi[par][here, h, tok].bitcast(F32), op0=ALU.mult, op1=ALU.subtract)
                    else:
                        last = nc.vector.tensor_tensor(k_st[par][there, h, tok], x_ps[bank][here, :],
                                                       k_st[par][here, h, tok].bitcast(F32), ALU.subtract)
                last.then_inc(x_free[bank], 1)

            def split_w(par, count):
                dve.wait_ge(w_hi_done, count)
                nc.vector.tensor_tensor(w_lo[par][:, :], w_raw[par][:, :], w_hi[par][:, :].bitcast(F32),
                                        ALU.subtract).then_inc(w_lo_done, 1)

            def reciprocals(t, u):
                done = unit_no(t, u)
                dve.wait_ge(exp_done, step_no(t, u, 0))
                nc.vector.reciprocal(recip[:, :], row_sum[:, (u - 1) % 2, :]).then_inc(recip_chain, 1)
                dve.wait_ge(recip_chain, done)
                nc.vector.tensor_copy(recip_wide[:, :, :], recip[:, :].unsqueeze(2).to_broadcast([P, 8, DH]))\
                  .then_inc(recip_ready, 1)

            def normalise(t, key, done):
                dve.wait_ge(pv_done, done)
                dve.wait_ge(m_free, M_USES.upto(t, key))
                nc.vector.tensor_tensor(z[:, :], z_ps[:, :], recip_t[:, :], ALU.mult).then_inc(z_done, 1)

            def add_output(t, key, tok):
                dve.wait_ge(m_full, M_USES.upto(t, key))
                nc.vector.tensor_tensor(s_t[:, tok], m_ps[:, :], s_t[:, tok], ALU.add).then_inc(m_free, 1)

            def copy_v(bank, k):
                return nc.vector.tensor_copy(v_quad[:, :, 2 * k:2 * k + 2, :],
                                             bank[:, :].rearrange("p (j r f) -> p r j f", j=2, r=2))

            def batch_stats(b):
                dve.wait_ge(x_in[b], 16)
                for i in range(b * SEQ_TILES, (b + 1) * SEQ_TILES):
                    nc.vector.bn_stats(stats[:, i, :], x_nat[:, i, :]).then_inc(stats_done, 1)

            def variances(tiles):
                dve.wait_ge(stats_done, tiles[-1] + 1)
                for i in tiles:
                    last = nc.vector.bn_aggr(mean_var[:, i, :], stats[:, i, :])
                last.then_inc(var_ready, 1)

            def inverse_std(part, tiles):
                dve.wait_ge(std_ready, part + 1)
                nc.vector.reciprocal(rstd[:, tiles], rstd[:, tiles]).then_inc(rstd_ready, 1)

            batch_stats(0)
            variances(range(SEQ_TILES))
            split_w(0, 1)
            inverse_std(0, slice(0, SEQ_TILES))
            dve.wait_ge(rstd_ready, 1)
            for i in range(SEQ_TILES):
                nc.vector.tensor_scalar(x_nat[:, i, :], x_nat[:, i, :], mean_var[:, i, 0:1], rstd[:, i:i + 1],
                                        ALU.subtract, ALU.mult).then_inc(xn_ready[0], 1)
            for n in (0, 1):
                dve.wait_ge(xt_hi, n + 1)
                tok = slice(n * BANK, (n + 1) * BANK)
                nc.vector.tensor_tensor(xl[:, tok], turned[n][:, :], xh[:, tok].bitcast(F32), ALU.subtract)\
                  .then_inc(xt_lo, 1)
            for blk in (0, 1):
                for s in (2 * blk, 2 * blk + 1):
                    project_lo(0, s, blk)
                    if s < BATCHES - 1:
                        batch_stats(s + 1)
                dve.wait_ge(v_full, blk + 1)
                copy_v(z_ps, 2 * blk + 1).then_inc(v_free, 1)
            variances(range(SEQ_TILES, TILES))
            inverse_std(1, slice(SEQ_TILES, TILES))
            row_max(Turn(0, "first"), 0, 0)
            split_w(1, 2)
            dve.wait_ge(w1_hi_done, 1)
            nc.vector.tensor_tensor(w1_lo[:, :], w1_raw[:, :], w1_hi[:, :].bitcast(F32), ALU.subtract)\
              .then_inc(w1_done, 1)
            nc.vector.tensor_scalar(b2_sb[:, 1:2], b2_sb[:, 0:1], -1.0, None, ALU.mult).then_inc(b2_done, 1)
            dve.wait_ge(s_zeroed[0], 1)

            def body(t):
                for u in range(4):
                    par, blk = u // 2, u % 2
                    for n in range(8):
                        if nxt := ahead(t, u, n):
                            row_max(*nxt)
                        for f in fillers("DVE", t, u, n):
                            if f[0] == "prep":
                                project_lo(1 - par, f[1], preps_before(t, u, f[1]))
                            if f[0] == "N":
                                reciprocals(t, u)
                            if f[0] == "Z":
                                since = (t, (u - 1, "R")) if u else (Turn(t.it - 1, "mid"), (3, "R"))
                                normalise(*since, unit_no(t, u) - 1)
                            if f[0] == "O":
                                quad = t.it if u >= 2 else t.it - 1
                                add_output(t, (u, "O"), bass.ds(batch_of(quad) * SEQ + (u % 2) * BANK, BANK))
                            if f == ("W1", 1):
                                dve.wait_ge(m_full, M_USES.upto(t, (u,) + f))
                                for c in (2, 3):
                                    last = nc.vector.tensor_scalar(h_sb[:, c, :], m_ps[:, (c - 2) * FT:(c - 1) * FT],
                                                                   b1_sb[:, c:c + 1], 0.0, ALU.add, ALU.max)
                                last.then_inc(m_free, 1)
                            if f[0] == "G":
                                dve.wait_ge(gate_exp, t.it + 1)
                                nc.vector.tensor_scalar(sig[:, 1, :], sig[:, 0, :], 1.0, None, ALU.add)\
                                  .then_inc(gate_chain, 1)
                                dve.wait_ge(gate_chain, t.it * 2 + 1)
                                nc.vector.reciprocal(sig[:, 0, :], sig[:, 1, :]).then_inc(gate_chain, 1)
                                dve.wait_ge(gate_chain, t.it * 2 + 2)
                                nc.vector.scalar_tensor_tensor(
                                    out=g_t[:, bass.ds(t.it * FT, FT)], in0=m_ps[:, 0:FT], scalar=b2_sb[:, 0:1],
                                    in1=sig[:, 0, :], op0=ALU.add, op1=ALU.mult).then_inc(m_free, 1)
                            if f[0] == "V" and f[1] % 2 == 1:
                                dve.wait_ge(m_full, M_USES.upto(t, (u,) + f))
                                dve.wait_ge(v_copied, t.it + 1)
                                copy_v(m_ps, f[1]).then_inc(m_free, 1)
                            if f[0] == "split":
                                split_w(f[1], t.it * 2 + (3 + f[1]))
                            if f[0] == "X":
                                tok = slice(f[1] * BANK, (f[1] + 1) * BANK)
                                dve.wait_ge(xt_hi, f[1] + 1)
                                nc.vector.tensor_tensor(s_t[:, tok].bitcast(F32R), m_ps[:, :], g_t[:, tok],
                                                        ALU.subtract).then_inc(m_free, 1)
                        if old := back(t, u, n, 1):
                            copy_turned(*old)
                if t.kind == "first":
                    dve.wait_ge(s_zeroed[1], 1)

            run(dve, body)
            copy_turned(Turn(QUADS - 1, "last"), 3, 7)
            normalise(Turn(QUADS - 1, "last"), (3, "R"), unit_no(END, 0) - 1)
            reciprocals(END, 0)
            add_output(END, "O before", bass.ds(TOKENS - SEQ, BANK))
            normalise(END, "R", unit_no(END, 0))
            add_output(END, "O", bass.ds(TOKENS - BANK, BANK))
            tok = slice(TOKENS - BANK, TOKENS)
            dve.wait_ge(xt_in, 16 * BATCHES)
            dve.wait_ge(m_free, M_USES.upto(END, "O"))
            nc.vector.tensor_tensor(s_t[:, tok], s_t[:, tok], g_t[:, tok], ALU.mult).then_inc(fin_chain, 1)
            dve.wait_ge(fin_chain, 1)
            nc.vector.tensor_tensor(g_t[:, tok], s_t[:, tok], x_t_sb[:, BANK:2 * BANK], ALU.add)\
              .then_inc(fin_ready, 1)


def kernel(L0_attn_x, L0_attn_W_K, L0_attn_W_Q, L0_attn_W_V, L0_attn_W_O, L0_ffn_W1, L0_ffn_b1,
           L0_ffn_W2, L0_ffn_b2):
    import numpy as np
    import concourse.bacc as bacc
    from concourse.bass_utils import run_bass_kernel_spmd

    lay = np.ascontiguousarray
    batches, seq, d = L0_attn_x.shape
    x = lay(np.asarray(L0_attn_x).reshape(batches * seq, d))
    feature_major = lambda w: lay(np.asarray(w).reshape(-1, d).T)
    arrays = {
        "x": x, "x_t": lay(x.T),
        "wq_t": feature_major(L0_attn_W_Q), "wk_t": feature_major(L0_attn_W_K),
        "wv_t": feature_major(L0_attn_W_V), "wo_t": lay(np.asarray(L0_attn_W_O).T),
        "w1": lay(L0_ffn_W1), "b1": lay(L0_ffn_b1), "w2": lay(L0_ffn_W2), "b2": lay(L0_ffn_b2),
    }
    nc = bacc.Bacc("TRN2", target_bir_lowering=False, num_devices=1)
    args = [nc.dram_tensor(name, a.shape, F32, kind="ExternalInput").ap() for name, a in arrays.items()]
    out_t = nc.dram_tensor("out_t", (d, batches * seq), F32, kind="ExternalOutput").ap()
    attention_gated_by_ffn(nc, *args, out_t)
    done = run_bass_kernel_spmd(nc, [arrays], core_ids=[0])
    return lay(done.results[0]["out_t"].T).reshape(batches, seq, d)
```
